# Optimizing a Trainium2 kernel written in Bass

```python
import numpy as np
import jax
import jax.numpy as jnp

def _softmax(x, axis=-1):
    return jax.nn.softmax(x, axis=axis)

def _gelu(x):
    return jax.nn.gelu(x, approximate=True)

def _silu(x):
    return jax.nn.silu(x)

def _sigmoid(x):
    return jax.nn.sigmoid(x)

def _layernorm(x, axis=-1, eps=1e-05):
    m = jnp.mean(x, axis=axis, keepdims=True)
    v = jnp.var(x, axis=axis, keepdims=True)
    return (x - m) / jnp.sqrt(v + eps)

def _scatter_add(tgt, idx, src, axis=0):
    return tgt.at[idx].add(src)

def _segment_sum(src, seg, n):
    return jax.ops.segment_sum(src, seg, n)
kernel_name = 'mk_rec_standalone_d1_rec_r8_e2d238'

def setup_inputs(seed: int=0):
    np.random.seed(seed)
    _w = jnp.asarray

    def _rec_inputs():
        import jax
        import jax.numpy as jnp
        _rk = jax.random.key(seed)
        r_inputs = jnp.stack([jax.random.randint(jax.random.fold_in(jax.random.fold_in(_rk, 1), 0), (2048,), 0, 99999, jnp.int32), jax.random.randint(jax.random.fold_in(jax.random.fold_in(_rk, 1), 1), (2048,), 0, 12499, jnp.int32), jax.random.randint(jax.random.fold_in(jax.random.fold_in(_rk, 1), 2), (2048,), 4, 99997, jnp.int32), jax.random.randint(jax.random.fold_in(jax.random.fold_in(_rk, 1), 3), (2048,), 2, 99997, jnp.int32), jax.random.randint(jax.random.fold_in(jax.random.fold_in(_rk, 1), 4), (2048,), 1, 99988, jnp.int32), jax.random.randint(jax.random.fold_in(jax.random.fold_in(_rk, 1), 5), (2048,), 1, 99996, jnp.int32), jax.random.randint(jax.random.fold_in(jax.random.fold_in(_rk, 1), 6), (2048,), 12, 99997, jnp.int32), jax.random.randint(jax.random.fold_in(jax.random.fold_in(_rk, 1), 7), (2048,), 17, 99995, jnp.int32), jax.random.randint(jax.random.fold_in(jax.random.fold_in(_rk, 1), 8), (2048,), 0, 99998, jnp.int32), jax.random.randint(jax.random.fold_in(jax.random.fold_in(_rk, 1), 9), (2048,), 0, 99998, jnp.int32), jax.random.randint(jax.random.fold_in(jax.random.fold_in(_rk, 1), 10), (2048,), 3, 99993, jnp.int32), jax.random.randint(jax.random.fold_in(jax.random.fold_in(_rk, 1), 11), (2048,), 0, 99993, jnp.int32), jax.random.randint(jax.random.fold_in(jax.random.fold_in(_rk, 1), 12), (2048,), 1, 99988, jnp.int32), jax.random.randint(jax.random.fold_in(jax.random.fold_in(_rk, 1), 13), (2048,), 0, 99997, jnp.int32), jax.random.randint(jax.random.fold_in(jax.random.fold_in(_rk, 1), 14), (2048,), 3, 99993, jnp.int32), jax.random.randint(jax.random.fold_in(jax.random.fold_in(_rk, 1), 15), (2048,), 10, 99994, jnp.int32), jax.random.randint(jax.random.fold_in(jax.random.fold_in(_rk, 1), 16), (2048,), 10, 99998, jnp.int32), jax.random.randint(jax.random.fold_in(jax.random.fold_in(_rk, 1), 17), (2048,), 18, 99979, jnp.int32), jax.random.randint(jax.random.fold_in(jax.random.fold_in(_rk, 1), 18), (2048,), 1, 99996, jnp.int32), jax.random.randint(jax.random.fold_in(jax.random.fold_in(_rk, 1), 19), (2048,), 6, 99987, jnp.int32), jax.random.randint(jax.random.fold_in(jax.random.fold_in(_rk, 1), 20), (2048,), 6, 12500, jnp.int32), jax.random.randint(jax.random.fold_in(jax.random.fold_in(_rk, 1), 21), (2048,), 2, 12500, jnp.int32), jax.random.randint(jax.random.fold_in(jax.random.fold_in(_rk, 1), 22), (2048,), 7, 12498, jnp.int32), jax.random.randint(jax.random.fold_in(jax.random.fold_in(_rk, 1), 23), (2048,), 2, 99999, jnp.int32), jax.random.randint(jax.random.fold_in(jax.random.fold_in(_rk, 1), 24), (2048,), 29, 99990, jnp.int32), jax.random.randint(jax.random.fold_in(jax.random.fold_in(_rk, 1), 25), (2048,), 10, 99986, jnp.int32)], axis=1)
        return r_inputs
    r_inputs = _rec_inputs()

    def _L0_rec_setup():
        import jax, jax.numpy as jnp
        import numpy as np
        N_FEAT = 26
        VOCAB = 12500
        EMBED = 64
        OUT = 256
        BATCH = 2048
        key = jax.random.key(seed)
        ks = jax.random.split(key, 9)
        inputs = jax.random.randint(ks[0], (BATCH, N_FEAT), 0, VOCAB)
        tables = jax.random.normal(ks[1], (N_FEAT, VOCAB, EMBED), dtype=jnp.float32) * 0.05
        lin_w = jax.random.normal(ks[2], (N_FEAT * EMBED, OUT), dtype=jnp.float32) * 0.02
        lin_b = jnp.zeros((OUT,), dtype=jnp.float32)
        inner_w = jax.random.normal(ks[3], (OUT, N_FEAT), dtype=jnp.float32)
        w1 = jax.random.normal(ks[4], (OUT * 2, 32), dtype=jnp.float32) * 0.05
        b1 = jnp.zeros((32,), dtype=jnp.float32)
        w2 = jax.random.normal(ks[5], (32, 1), dtype=jnp.float32) * 0.1
        b2 = jnp.zeros((1,), dtype=jnp.float32)
        return {'inputs': inputs, 'tables': tables, 'lin_w': lin_w, 'lin_b': lin_b, 'inner_w': inner_w, 'w1': w1, 'b1': b1, 'w2': w2, 'b2': b2}
    _L0_rec_all = _L0_rec_setup()
    _L0_rec_in = {k: v for k, v in _L0_rec_all.items() if k in ('tables', 'lin_w', 'lin_b', 'inner_w', 'w1', 'b1', 'w2', 'b2')}
    del _L0_rec_all
    return {'r_inputs': r_inputs, 'L0_rec_tables': _L0_rec_in['tables'], 'L0_rec_lin_w': _L0_rec_in['lin_w'], 'L0_rec_lin_b': _L0_rec_in['lin_b'], 'L0_rec_inner_w': _L0_rec_in['inner_w'], 'L0_rec_w1': _L0_rec_in['w1'], 'L0_rec_b1': _L0_rec_in['b1'], 'L0_rec_w2': _L0_rec_in['w2'], 'L0_rec_b2': _L0_rec_in['b2']}

def reference(r_inputs, L0_rec_tables, L0_rec_lin_w, L0_rec_lin_b, L0_rec_inner_w, L0_rec_w1, L0_rec_b1, L0_rec_w2, L0_rec_b2):
    import jax
    import jax.numpy as jnp

    def _L0_rec_ref(inputs, tables, lin_w, lin_b, inner_w, w1, b1, w2, b2):
        import jax, jax.numpy as jnp
        import numpy as np
        N_FEAT = 26
        VOCAB = 12500
        EMBED = 64
        OUT = 256
        BATCH = 2048
        B = inputs.shape[0]
        emb = tables[jnp.arange(N_FEAT)[None, :], inputs]
        flat = emb.reshape(B, N_FEAT * EMBED)
        lz = flat @ lin_w + lin_b
        delta = jnp.einsum('bfe,of->boe', emb, inner_w)
        lp = jnp.sqrt(jnp.sum(delta * delta, axis=-1))
        prod_out = jnp.concatenate([lz, lp], axis=1)
        h = jax.nn.relu(prod_out @ w1 + b1)
        return jax.nn.sigmoid(h @ w2 + b2)
    y = _L0_rec_ref(r_inputs, L0_rec_tables, L0_rec_lin_w, L0_rec_lin_b, L0_rec_inner_w, L0_rec_w1, L0_rec_b1, L0_rec_w2, L0_rec_b2)
    return y

_drawn_inputs = setup_inputs


def setup_inputs(seed=0):
    import zlib

    import numpy as np

    out = dict(_drawn_inputs(seed))
    spreads = {'L0_rec_lin_b': (0.0, 2.0), 'L0_rec_b1': (0.0, 2.0)}
    factors = {'L0_rec_tables': 26.32, 'L0_rec_lin_w': 64.0, 'L0_rec_w1': 36.2, 'L0_rec_inner_w': 8.0}
    for name, (base, spread) in spreads.items():
        noise = np.random.default_rng([zlib.crc32(name.encode()), seed]).standard_normal(out[name].shape)
        drawn = base * np.exp(spread * noise) if base else spread * noise
        out[name] = jnp.asarray(drawn.astype(out[name].dtype))
    for name, factor in factors.items():
        out[name] = (out[name] * factor).astype(out[name].dtype)
    return out
```

```python
import concourse.bass as bass
from concourse import mybir
from contextlib import ExitStack


def product_network_kernel(
    nc: bass.Bass,
    r_inputs: bass.AP,
    tables: bass.AP,
    lin_w: bass.AP,
    lin_b: bass.AP,
    inner_w: bass.AP,
    w1: bass.AP,
    b1: bass.AP,
    w2: bass.AP,
    b2: bass.AP,
    out: bass.AP,
):
    fp32 = mybir.dt.float32
    i32 = mybir.dt.int32
    u32 = mybir.dt.uint32
    ALU = mybir.AluOpType
    ACT = mybir.ActivationFunctionType
    AX_X = mybir.AxisListType.X

    B, F = r_inputs.shape
    _, V, E = tables.shape
    O = inner_w.shape[0]
    HID = w1.shape[1]
    P = 128
    TILES = B // P
    RG = 32
    Q = P // RG
    R = F * Q
    EG = E // Q
    OH = O // P
    BANK = 512
    GRP = BANK // P
    GRPS = EG // GRP
    PAIRS = Q // 2
    STEPS = OH * GRPS * PAIRS
    STEP_COLS = 2 * BANK
    CHUNKS = 4
    CH_STEPS = STEPS // CHUNKS
    CH_COLS = CH_STEPS * STEP_COLS
    GATHER = 16 * F
    LIN_AT = STEPS // GRPS

    table_rows = tables.rearrange("f v e -> (f v) e")
    idx_dram = r_inputs.rearrange("(p t) f -> p (t f)", p=P)
    out_dram = out.rearrange("(p t) o -> p (t o)", p=P)
    lin_dram = lin_w.rearrange("(r g) o -> r g o", g=EG)

    ctx = ExitStack()
    with ctx:
        def sb(name, shape, dt=fp32):
            return ctx.enter_context(nc.sbuf_tensor(name, shape, dt))

        def sem(name):
            return ctx.enter_context(nc.semaphore(name))

        idx_raw = sb("idx_raw", [P, TILES * F], i32)
        idx_lim = sb("idx_lim", [P, TILES * F])
        idx_neg = sb("idx_neg", [P, TILES * F])
        idx_row = sb("idx_row", [P, TILES, F], u32)
        feat_row = sb("feat_row", [P, TILES * F], i32)
        idx_stage = sb("idx_stage", [P, 2, F], u32)
        emb = [sb(f"emb{s}", [P, F, E]) for s in range(2)]
        embT = [sb(f"embT{s}", [R, EG, P]) for s in range(2)]
        embG = [sb(f"embG{s}", [P, EG, P]) for s in range(2)]
        squares = sb("squares", [P, CHUNKS, CH_COLS])
        part_sum = sb("part_sum", [P, CHUNKS, P])
        sq_sum = sb("sq_sum", [P, OH, P])
        lp = sb("lp", [P, 2, OH, P])
        hid = sb("hid", [HID + 1, 2, P])
        y_all = sb("y_all", [P, TILES])
        y_sig = sb("y_sig", [P, TILES])
        ident = sb("ident", [P, P])
        inner_sb = sb("inner_sb", [P, OH, F])
        inner_rep = sb("inner_rep", [P, OH, Q, RG])
        innerT = sb("innerT", [P, OH, P])
        lin_sb = sb("lin_sb", [R, EG, O])
        linT = sb("linT", [P, 2, 2, OH, R])
        fold = sb("fold", [R, EG, HID])
        w1_sb = sb("w1_sb", [P, 2 * OH, HID])
        lin_b_sb = sb("lin_b_sb", [P, OH])
        b1_sb = sb("b1_sb", [HID, 1])
        hid_bias = sb("hid_bias", [HID, 1])
        w2_sb = sb("w2_sb", [HID + 1, 1])

        delta = [ctx.enter_context(nc.psum_tensor(f"delta{i}", [P, STEP_COLS], fp32)) for i in range(2)]
        turned = [ctx.enter_context(nc.psum_tensor(f"turned{i}", [P, BANK], fp32)) for i in range(2)]
        head = [ctx.enter_context(nc.psum_tensor(f"head{i}", [P, BANK], fp32)) for i in range(2)]
        pre_h = [head[s][0:HID, 0:P] for s in range(2)]
        y_ps = [head[s][:, P:P + 1] for s in range(2)]
        bias_ps = head[0][0:HID, 0:1]

        idx_loaded = sem("idx_loaded")
        inner_loaded = sem("inner_loaded")
        lin_loaded = sem("lin_loaded")
        small_loaded = sem("small_loaded")
        feat_ready = sem("feat_ready")
        ident_ready = sem("ident_ready")
        ident_zero = sem("ident_zero")
        idx_limited = sem("idx_limited")
        idx_based = sem("idx_based")
        rows_ready = sem("rows_ready")
        rep_zeroed = sem("rep_zeroed")
        rep_ready = sem("rep_ready")
        inner_turned = sem("inner_turned")
        innerT_ready = sem("innerT_ready")
        lin_turned = sem("lin_turned")
        linT_ready = sem("linT_ready")
        fold_done = sem("fold_done")
        fold_ready = sem("fold_ready")
        bias_done = sem("bias_done")
        bias_ready = sem("bias_ready")
        ones_ready = sem("ones_ready")
        staged = sem("staged")
        gather_begun = sem("gather_begun")
        gathered = [sem(f"gathered{s}") for s in range(2)]
        tile_turned = sem("tile_turned")
        embT_ready = sem("embT_ready")
        regrouped = [[sem(f"regrouped{s}_{m}") for m in range(2)] for s in range(2)]
        delta_done = sem("delta_done")
        squared = sem("squared")
        chunk_summed = sem("chunk_summed")
        half_summed = sem("half_summed")
        lp_ready = sem("lp_ready")
        linear_done = sem("linear_done")
        pre_h_done = sem("pre_h_done")
        hid_ready = sem("hid_ready")
        y_done = sem("y_done")
        y_kept = sem("y_kept")
        sig_ready = sem("sig_ready")
        out_stored = sem("out_stored")

        block = ctx.enter_context(nc.Block())

        @block.sync
        def _(sp):
            sp.dma_start(idx_raw[:, :], idx_dram).then_inc(idx_loaded, 16)
            sp.dma_start(inner_sb[:, :, :], inner_w.rearrange("(p h) f -> p h f", h=OH)).then_inc(inner_loaded, 16)
            sp.dma_start(w1_sb[:, :, :].rearrange("p (c h) n -> p c h n", h=OH),
                         w1.rearrange("(c p h) n -> p c h n", p=P, h=OH)).then_inc(small_loaded, 16)
            sp.dma_start(lin_b_sb[:, :], lin_b.rearrange("(p h) -> p h", h=OH)).then_inc(small_loaded, 16)
            sp.dma_start(b1_sb[:, :], b1.rearrange("(p o) -> p o", o=1)).then_inc(small_loaded, 16)
            sp.dma_start(w2_sb[0:HID, :], w2).then_inc(small_loaded, 16)
            sp.dma_start(w2_sb[HID:HID + 1, :], b2.rearrange("(p o) -> p o", o=1)).then_inc(small_loaded, 16)
            sp.dma_start(lin_sb[:, :, :], lin_dram).then_inc(lin_loaded, 16)

            def regroup_tile(j, s, first_use):
                t = j * 2 + s
                for m in range(2):
                    sp.wait_ge(embT_ready, t * GRPS + (m + 1) * GRPS // 2)
                    if m == 0 and not first_use:
                        sp.wait_ge(delta_done, t * STEPS - STEPS)
                    for q in range(Q):
                        half = slice(m * EG // 2, (m + 1) * EG // 2)
                        sp.dma_start(embG[s][q * RG:q * RG + F, half, :],
                                     embT[s][q::Q, half, :]).then_inc(regrouped[s][m], 16)

            regroup_tile(0, 0, True)
            regroup_tile(0, 1, True)
            with sp.Fori(1, TILES // 2) as j:
                regroup_tile(j, 0, False)
                regroup_tile(j, 1, False)
            sp.wait_ge(sig_ready, 1)
            sp.dma_start(out_dram, y_sig[:, :]).then_inc(out_stored, 16)
            sp.wait_ge(out_stored, 16)

        @block.gpsimd
        def _(pool):
            nc.gpsimd.iota(feat_row[:, :].rearrange("p (t f) -> p t f", f=F), [[0, TILES], [V, F]],
                           base=0, channel_multiplier=0).then_inc(feat_ready, 1)
            nc.gpsimd.memset(ident[:, :], 0.0).then_inc(ident_zero, 1)
            pool.wait_ge(ident_zero, 1)
            nc.gpsimd.affine_select(out=ident[:, :], in_=ident[:, :], compare_op=ALU.not_equal, fill=1.0,
                                    base=0, pattern=[[-1, P]], channel_multiplier=1).then_inc(ident_ready, 1)

            def gather_tile(j, s, first_use):
                pool.wait_ge(staged, j * 2 + (s + 1))
                if not first_use:
                    pool.wait_ge(tile_turned, (j * 2 + s - 1) * GRPS)
                pool.sem_inc(gather_begun, 1)
                for f in range(F):
                    nc.gpsimd.indirect_dma_start(
                        emb[s][:, f, :], None, table_rows,
                        bass.IndirectOffsetOnAxis(ap=idx_stage[:, s, f:f + 1], axis=0)).then_inc(gathered[s], 16)

            gather_tile(0, 0, True)
            gather_tile(0, 1, True)
            with pool.Fori(1, TILES // 2) as j:
                gather_tile(j, 0, False)
                gather_tile(j, 1, False)

        @block.tensor
        def _(pe):
            pe.wait_ge(ident_ready, 1)
            pe.wait_ge(rep_ready, 1)
            for h in range(OH):
                last = nc.tensor.transpose(turned[0][:, h * P:(h + 1) * P],
                                           inner_rep[:, h, :, :].rearrange("p q f -> p (q f)"), ident[:, :])
            last.then_inc(inner_turned, 1)
            pe.wait_ge(small_loaded, 16 * 5)
            for h in range(OH):
                last = nc.tensor.matmul(bias_ps, w1_sb[:, h, :], lin_b_sb[:, h:h + 1],
                                        start=(h == 0), stop=(h == OH - 1))
            last.then_inc(bias_done, 1)
            pe.wait_ge(lin_loaded, 16)

            def fold_products(i):
                pe.wait_ge(linT_ready, i + 1)
                for g in range(2):
                    for h in range(OH):
                        nc_last = nc.tensor.matmul(head[1][0:R, (2 * i + g) * HID:(2 * i + g + 1) * HID],
                                                   linT[:, i % 2, g, h, :], w1_sb[:, h, :],
                                                   start=(h == 0), stop=(h == OH - 1))
                nc_last.then_inc(fold_done, 1)

            for i in range(EG // 2):
                if i >= 2:
                    pe.wait_ge(linT_ready, i - 1)
                for g in range(2):
                    for h in range(OH):
                        c = (g * OH + h) * P
                        last = nc.tensor.transpose(delta[i % 2][:, c:c + R],
                                                   lin_sb[:, 2 * i + g, h::OH], ident[0:R, 0:R])
                last.then_inc(lin_turned, 1)
                if i >= 1:
                    fold_products(i - 1)
            fold_products(EG // 2 - 1)
            pe.wait_ge(fold_ready, 1)
            pe.wait_ge(bias_ready, 1)
            pe.wait_ge(innerT_ready, 1)

            def turn_tile(j, s):
                t = j * 2 + s
                pe.wait_ge(gathered[s], (j + 1) * GATHER)
                for k in range(GRPS):
                    if k >= 2:
                        pe.wait_ge(embT_ready, t * GRPS + (k - 1))
                    for g in range(GRP):
                        last = nc.tensor.transpose(
                            turned[k % 2][0:R, g * P:(g + 1) * P],
                            emb[s][:, :, :].rearrange("p f e -> p (f e)")[:, k * GRP + g::EG], ident[:, :])
                    last.then_inc(tile_turned, 1)

            def delta_step(j, s, step):
                t = j * 2 + s
                h, k, pair = step // (GRPS * PAIRS), step // PAIRS % GRPS, step % PAIRS
                if h == 0 and pair == 0 and k % (GRPS // 2) == 0:
                    m = k // (GRPS // 2)
                    pe.wait_ge(regrouped[s][m], (j + 1) * 16 * Q)
                if step >= 2:
                    pe.wait_ge(squared, t * STEPS + (step - 1))
                for i in range(2):
                    r = (pair * 2 + i) * RG
                    last = nc.tensor.matmul(delta[step % 2][:, i * BANK:(i + 1) * BANK],
                                            innerT[r:r + F, h, :],
                                            embG[s][r:r + F, k * GRP:(k + 1) * GRP, :].rearrange("p g b -> p (g b)"),
                                            start=True, stop=True)
                last.then_inc(delta_done, 1)

            def linear_part(s, k):
                for g in range(k * GRP, (k + 1) * GRP):
                    last = nc.tensor.matmul(pre_h[s], fold[:, g, :], embT[s][:, g, :],
                                            start=(g == 0), stop=False)
                return last

            def finish_lp(j, s):
                pe.wait_ge(lp_ready, j * 2 * OH + OH * (s + 1))
                for h in range(OH):
                    last = nc.tensor.matmul(pre_h[s], w1_sb[:, OH + h, :], lp[:, s, h, :],
                                            start=False, stop=(h == OH - 1))
                last.then_inc(pre_h_done, 1)

            def finish_y(j, s):
                pe.wait_ge(hid_ready, j * 2 + (s + 1))
                nc.tensor.matmul(y_ps[s], hid[:, s, :], w2_sb[:, :], start=True, stop=True).then_inc(y_done, 1)

            def tile(j, s, before):
                turn_tile(j, s)
                for step in range(STEPS):
                    delta_step(j, s, step)
                    if step % LIN_AT == LIN_AT - 1:
                        k = step // LIN_AT
                        last = linear_part(s, k)
                        if k == GRPS - 1:
                            last.then_inc(linear_done, 1)
                    if before is not None and step == 4:
                        finish_lp(*before)
                    if before is not None and step == 8:
                        finish_y(*before)

            tile(0, 0, None)
            tile(0, 1, (0, 0))
            with pe.Fori(1, TILES // 2) as j:
                tile(j, 0, (j - 1, 1))
                tile(j, 1, (j, 0))
            finish_lp(TILES // 2 - 1, 1)
            finish_y(TILES // 2 - 1, 1)

        @block.scalar
        def _(act):
            act.wait_ge(inner_turned, 1)
            nc.scalar.copy(innerT[:, :, :].rearrange("p h o -> p (h o)"),
                           turned[0][:, 0:OH * P]).then_inc(innerT_ready, 1)
            for i in range(EG // 2):
                act.wait_ge(lin_turned, i + 1)
                if i >= 2:
                    act.wait_ge(fold_done, i - 1)
                nc.scalar.copy(linT[:, i % 2, :, :, :].rearrange("p g h c -> p (g h) c"),
                               delta[i % 2][:, 0:2 * OH * P].rearrange("p (n c) -> p n c", c=P)[:, :, 0:R]).then_inc(linT_ready, 1)

            def keep_turned(j, s, k):
                t = j * 2 + s
                act.wait_ge(tile_turned, t * GRPS + (k + 1))
                nc.scalar.copy(embT[s][:, k * GRP:(k + 1) * GRP, :].rearrange("p g b -> p (g b)"),
                               turned[k % 2][0:R, :]).then_inc(embT_ready, 1)

            def square_step(j, s, step, first_tile):
                t = j * 2 + s
                chunk = step // CH_STEPS
                act.wait_ge(delta_done, t * STEPS + (step + 1))
                if not first_tile and step % CH_STEPS == 0:
                    act.wait_ge(chunk_summed, t * CHUNKS + (chunk + 1 - CHUNKS))
                c = step % CH_STEPS * STEP_COLS
                nc.scalar.activation(squares[:, chunk, c:c + STEP_COLS], delta[step % 2][:, :],
                                     ACT.Square).then_inc(squared, 1)

            def root(j, s, h):
                t = j * 2 + s
                act.wait_ge(half_summed, t * OH + (h + 1))
                nc.scalar.activation(lp[:, s, h, :], sq_sum[:, h, :], ACT.Sqrt).then_inc(lp_ready, 1)

            def tile(j, s, before, first_use):
                if not first_use:
                    act.wait_ge(linear_done, j * 2 + s - 1)
                for k in range(GRPS):
                    keep_turned(j, s, k)
                if before is not None:
                    root(*before, OH - 1)
                for step in range(STEPS):
                    square_step(j, s, step, before is None)
                    if step == 3 * STEPS // 4 - 1:
                        if not first_use:
                            act.wait_ge(pre_h_done, j * 2 + s - 1)
                        root(j, s, 0)

            tile(0, 0, None, True)
            tile(0, 1, (0, 0), True)
            with act.Fori(1, TILES // 2) as j:
                tile(j, 0, (j - 1, 1), False)
                tile(j, 1, (j, 0), False)
            root(TILES // 2 - 1, 1, OH - 1)
            act.wait_ge(y_kept, TILES)
            nc.scalar.activation(y_sig[:, :], y_all[:, :], ACT.Sigmoid).then_inc(sig_ready, 1)

        @block.vector
        def _(dve):
            dve.wait_ge(idx_loaded, 16)
            nc.vector.tensor_scalar(idx_lim[:, :], idx_raw[:, :], -V, V - 1, ALU.max, ALU.min).then_inc(idx_limited, 1)
            dve.wait_ge(idx_limited, 1)
            nc.vector.tensor_scalar(idx_neg[:, :], idx_lim[:, :], 0, V, ALU.is_lt, ALU.mult).then_inc(idx_based, 1)
            dve.wait_ge(idx_based, 1)
            nc.vector.tensor_tensor(idx_lim[:, :], idx_lim[:, :], idx_neg[:, :], ALU.add).then_inc(idx_based, 1)
            dve.wait_ge(idx_based, 2)
            dve.wait_ge(feat_ready, 1)
            nc.vector.tensor_tensor(idx_row[:, :, :].rearrange("p t f -> p (t f)"), idx_lim[:, :],
                                    feat_row[:, :], ALU.add).then_inc(rows_ready, 1)
            dve.wait_ge(rows_ready, 1)
            for s in range(2):
                nc.vector.tensor_copy(idx_stage[:, s, :], idx_row[:, s, :]).then_inc(staged, 1)
            nc.vector.memset(inner_rep[:, :, :, :], 0.0).then_inc(rep_zeroed, 1)
            nc.vector.memset(hid[HID:HID + 1, :, :], 1.0).then_inc(ones_ready, 1)
            dve.wait_ge(rep_zeroed, 1)
            dve.wait_ge(inner_loaded, 16)
            for q in range(Q):
                last = nc.vector.tensor_copy(inner_rep[:, :, q, 0:F], inner_sb[:, :, :])
            last.then_inc(rep_ready, 1)
            dve.wait_ge(bias_done, 1)
            nc.vector.tensor_tensor(hid_bias[:, :], bias_ps, b1_sb[:, :], ALU.add).then_inc(bias_ready, 1)
            dve.wait_ge(fold_done, EG // 2)
            nc.vector.tensor_copy(fold[:, :, :].rearrange("p g n -> p (g n)"), head[1][0:R, 0:EG * HID]).then_inc(fold_ready, 1)
            dve.wait_ge(bias_ready, 1)

            def sum_chunk(j, s, chunk, first_tile):
                t = j * 2 + s
                dve.wait_ge(squared, t * STEPS + CH_STEPS * (chunk + 1))
                nc.vector.tensor_reduce(part_sum[:, chunk, :], squares[:, chunk, :].rearrange("p (e b) -> p b e", b=P),
                                        AX_X, ALU.add).then_inc(chunk_summed, 1)
                if chunk % 2 == 1:
                    h = chunk // 2
                    dve.wait_ge(chunk_summed, t * CHUNKS + (chunk + 1))
                    if not first_tile:
                        dve.wait_ge(lp_ready, t * OH + (h + 1 - OH))
                    nc.vector.tensor_tensor(sq_sum[:, h, :], part_sum[:, chunk - 1, :], part_sum[:, chunk, :],
                                            ALU.add).then_inc(half_summed, 1)

            def relu(j, s):
                t = j * 2 + s
                dve.wait_ge(pre_h_done, t + 1)
                nc.vector.tensor_scalar(hid[0:HID, s, :], pre_h[s], hid_bias[:, :], 0.0,
                                        ALU.add, ALU.max).then_inc(hid_ready, 1)

            def keep_y(j, s):
                t = j * 2 + s
                dve.wait_ge(y_done, t + 1)
                nc.vector.tensor_copy(y_all[:, bass.ds(t, 1)], y_ps[s]).then_inc(y_kept, 1)

            def tile(j, s, before, stage_next):
                if stage_next:
                    dve.wait_ge(gathered[s], (j + 1) * GATHER)
                    nc.vector.tensor_copy(idx_stage[:, s, :],
                                          idx_row[:, bass.ds(j * 2 + (s + 2), 1), :].rearrange("p t f -> p (t f)")
                                          ).then_inc(staged, 1)
                for chunk in range(CHUNKS):
                    sum_chunk(j, s, chunk, before is None)
                    if chunk == 1 and before is not None:
                        relu(*before)
                    if chunk == 2 and before is not None:
                        keep_y(*before)

            tile(0, 0, None, True)
            tile(0, 1, (0, 0), True)
            with dve.Fori(1, TILES // 2 - 1) as j:
                tile(j, 0, (j - 1, 1), True)
                tile(j, 1, (j, 0), True)
            last_pair = TILES // 2 - 1
            tile(last_pair, 0, (last_pair - 1, 1), False)
            tile(last_pair, 1, (last_pair, 0), False)
            relu(last_pair, 1)
            keep_y(last_pair, 1)


_INS = ['r_inputs', 'L0_rec_tables', 'L0_rec_lin_w', 'L0_rec_lin_b', 'L0_rec_inner_w',
        'L0_rec_w1', 'L0_rec_b1', 'L0_rec_w2', 'L0_rec_b2']
_OUTS = [((2048, 1), 'float32')]


def kernel(**inputs):
    import numpy as _np
    import concourse.bacc as _bacc
    from concourse import mybir as _mybir
    from concourse.bass_utils import run_bass_kernel_spmd as _run

    nc = _bacc.Bacc("TRN2", target_bir_lowering=False, num_devices=1)
    arrays, args = {}, []
    for name in _INS:
        a = _np.ascontiguousarray(inputs[name])
        arrays[f"in_{name}_dram"] = a
        args.append(nc.dram_tensor(f"in_{name}_dram", a.shape, _mybir.dt.from_np(a.dtype), kind="ExternalInput").ap())
    for i, (shape, dtype) in enumerate(_OUTS):
        dt = _mybir.dt.from_np(_np.dtype(dtype))
        args.append(nc.dram_tensor(f"out_{i}_dram", shape, dt, kind="ExternalOutput").ap())
    product_network_kernel(nc, *args)
    r = _run(nc, [arrays], core_ids=[0])
    return r.results[0]["out_0_dram"]
```

```python
import concourse.bass as bass
from concourse import mybir
from contextlib import ExitStack


def product_network_kernel(
    nc: bass.Bass,
    r_inputs: bass.AP,
    tables: bass.AP,
    lin_w: bass.AP,
    lin_b: bass.AP,
    inner_w: bass.AP,
    w1: bass.AP,
    b1: bass.AP,
    w2: bass.AP,
    b2: bass.AP,
    out: bass.AP,
):
    fp32 = mybir.dt.float32
    fp32r = mybir.dt.float32r
    i32 = mybir.dt.int32
    u32 = mybir.dt.uint32
    ALU = mybir.AluOpType
    ACT = mybir.ActivationFunctionType
    AX_X = mybir.AxisListType.X

    B, F = r_inputs.shape
    _, V, E = tables.shape
    O = inner_w.shape[0]
    HID = w1.shape[1]
    P = 128
    TILES = B // P
    Q = 4
    EG = E // Q
    R = F * Q
    PARTS = 4
    K = PARTS * F
    OH = O // P
    BANK = 512
    GRP = BANK // P
    GRPS = EG // GRP
    STEP_COLS = 2 * BANK
    STEP_E = 2 * GRP
    CHUNKS = 4
    CH_STEPS = E // 2 // STEP_E
    STEPS = CHUNKS * CH_STEPS
    CH_COLS = CH_STEPS * STEP_COLS
    GATHER = 16 * F
    REGROUP = 16 * 2 * PARTS

    table_rows = tables.rearrange("f v e -> (f v) e")
    idx_dram = r_inputs.rearrange("(p t) f -> p (t f)", p=P)
    out_dram = out.rearrange("(p t) o -> p (t o)", p=P)
    lin_dram = lin_w.rearrange("(r g) o -> r g o", g=EG)

    ctx = ExitStack()
    with ctx:
        def sb(name, shape, dt=fp32):
            return ctx.enter_context(nc.sbuf_tensor(name, shape, dt))

        def sem(name):
            return ctx.enter_context(nc.semaphore(name))

        idx_raw = sb("idx_raw", [P, TILES * F], i32)
        idx_lim = sb("idx_lim", [P, TILES * F])
        idx_neg = sb("idx_neg", [P, TILES * F])
        idx_row = sb("idx_row", [P, TILES, F], u32)
        feat_row = sb("feat_row", [P, TILES * F], i32)
        idx_stage = sb("idx_stage", [P, 2, F], u32)
        emb = [sb(f"emb{s}", [P, F, E]) for s in range(2)]
        emb_hi = [sb(f"emb_hi{s}", [R, EG, P], fp32r) for s in range(2)]
        emb_lo = [sb(f"emb_lo{s}", [R, EG, P], fp32r) for s in range(2)]
        emb_parts = [sb(f"emb_parts{s}", [K, E, P], fp32r) for s in range(2)]
        squares = sb("squares", [P, CHUNKS, CH_COLS])
        part_sum = sb("part_sum", [P, CHUNKS, P])
        sq_sum = sb("sq_sum", [P, OH, P])
        lp = sb("lp", [P, 2, OH, P])
        hid = sb("hid", [HID + 1, 2, P])
        y_all = sb("y_all", [P, TILES])
        y_sig = sb("y_sig", [P, TILES])
        ident = sb("ident", [P, P])
        inner_sb = sb("inner_sb", [P, OH, F])
        inner_parts = sb("inner_parts", [P, OH, PARTS, F])
        innerT = sb("innerT", [K, OH, P], fp32r)
        lin_sb = squares[0:R, 0, :].rearrange("r (g o) -> r g o", o=O)
        linT = sb("linT", [P, 2, 2, OH, R])
        fold_hi = sb("fold_hi", [R, EG, HID], fp32r)
        fold_lo = sb("fold_lo", [R, EG, HID], fp32r)
        w1_sb = sb("w1_sb", [P, 2 * OH, HID])
        lin_b_sb = sb("lin_b_sb", [P, OH])
        b1_sb = sb("b1_sb", [HID, 1])
        hid_bias = sb("hid_bias", [HID, 1])
        w2_sb = sb("w2_sb", [HID + 1, 1])

        delta = [ctx.enter_context(nc.psum_tensor(f"delta{i}", [P, STEP_COLS], fp32)) for i in range(2)]
        turned = [ctx.enter_context(nc.psum_tensor(f"turned{i}", [P, BANK], fp32)) for i in range(2)]
        head = [ctx.enter_context(nc.psum_tensor(f"head{i}", [P, BANK], fp32)) for i in range(2)]
        pre_h = [head[s][0:HID, 0:P] for s in range(2)]
        y_ps = [head[s][:, P:P + 1] for s in range(2)]
        bias_ps = head[0][0:HID, 0:1]

        idx_loaded = sem("idx_loaded")
        inner_loaded = sem("inner_loaded")
        lin_loaded = sem("lin_loaded")
        small_loaded = sem("small_loaded")
        feat_ready = sem("feat_ready")
        ident_ready = sem("ident_ready")
        ident_zero = sem("ident_zero")
        idx_limited = sem("idx_limited")
        idx_based = sem("idx_based")
        rows_ready = sem("rows_ready")
        inner_high = sem("inner_high")
        inner_split = sem("inner_split")
        inner_turned = sem("inner_turned")
        innerT_ready = sem("innerT_ready")
        lin_turned = sem("lin_turned")
        linT_ready = sem("linT_ready")
        fold_done = sem("fold_done")
        fold_high = sem("fold_high")
        fold_ready = sem("fold_ready")
        bias_done = sem("bias_done")
        bias_ready = sem("bias_ready")
        ones_ready = sem("ones_ready")
        staged = sem("staged")
        gather_begun = sem("gather_begun")
        gathered = [sem(f"gathered{s}") for s in range(2)]
        tile_turned = sem("tile_turned")
        high_ready = sem("high_ready")
        low_ready = sem("low_ready")
        regrouped = [[sem(f"regrouped{s}_{m}") for m in range(2)] for s in range(2)]
        delta_done = sem("delta_done")
        squared = sem("squared")
        chunk_summed = sem("chunk_summed")
        half_summed = sem("half_summed")
        lp_ready = sem("lp_ready")
        linear_done = sem("linear_done")
        pre_h_done = sem("pre_h_done")
        hid_ready = sem("hid_ready")
        y_done = sem("y_done")
        y_kept = sem("y_kept")
        sig_ready = sem("sig_ready")
        out_stored = sem("out_stored")

        def count(j, s, each, more):
            return j * (2 * each) + (s * each + more)

        block = ctx.enter_context(nc.Block())

        @block.sync
        def _(sp):
            sp.dma_start(idx_raw[:, :], idx_dram).then_inc(idx_loaded, 16)
            sp.dma_start(inner_sb[:, :, :], inner_w.rearrange("(p h) f -> p h f", h=OH)).then_inc(inner_loaded, 16)
            sp.dma_start(w1_sb[:, :, :].rearrange("p (c h) n -> p c h n", h=OH),
                         w1.rearrange("(c p h) n -> p c h n", p=P, h=OH)).then_inc(small_loaded, 16)
            sp.dma_start(lin_b_sb[:, :], lin_b.rearrange("(p h) -> p h", h=OH)).then_inc(small_loaded, 16)
            sp.dma_start(b1_sb[:, :], b1.rearrange("(p o) -> p o", o=1)).then_inc(small_loaded, 16)
            sp.dma_start(w2_sb[0:HID, :], w2).then_inc(small_loaded, 16)
            sp.dma_start(w2_sb[HID:HID + 1, :], b2.rearrange("(p o) -> p o", o=1)).then_inc(small_loaded, 16)
            sp.dma_start(lin_sb[:, :, :], lin_dram).then_inc(lin_loaded, 16)

            def regroup_tile(j, s, first_use):
                sp.wait_ge(low_ready, count(j, s, GRPS, GRPS))
                if not first_use:
                    sp.wait_ge(delta_done, count(j, s, STEPS, -STEPS))
                for q in range(Q):
                    for part in range(PARTS):
                        src = (emb_hi, emb_lo)[part % 2][s]
                        sp.dma_start(emb_parts[s][part * F:(part + 1) * F, q * EG:(q + 1) * EG, :].bitcast(fp32),
                                     src[q::Q, :, :].bitcast(fp32)).then_inc(regrouped[s][q // 2], 16)

            regroup_tile(0, 0, True)
            regroup_tile(0, 1, True)
            with sp.Fori(1, TILES // 2) as j:
                regroup_tile(j, 0, False)
                regroup_tile(j, 1, False)
            sp.wait_ge(sig_ready, 1)
            sp.dma_start(out_dram, y_sig[:, :]).then_inc(out_stored, 16)
            sp.wait_ge(out_stored, 16)

        @block.gpsimd
        def _(pool):
            nc.gpsimd.iota(feat_row[:, :].rearrange("p (t f) -> p t f", f=F), [[0, TILES], [V, F]],
                           base=0, channel_multiplier=0).then_inc(feat_ready, 1)
            nc.gpsimd.memset(ident[:, :], 0.0).then_inc(ident_zero, 1)
            pool.wait_ge(ident_zero, 1)
            nc.gpsimd.affine_select(out=ident[:, :], in_=ident[:, :], compare_op=ALU.not_equal, fill=1.0,
                                    base=0, pattern=[[-1, P]], channel_multiplier=1).then_inc(ident_ready, 1)

            def gather_tile(j, s, first_use):
                pool.wait_ge(staged, count(j, s, 1, 1))
                if not first_use:
                    pool.wait_ge(tile_turned, count(j, s, GRPS, -GRPS))
                pool.sem_inc(gather_begun, 1)
                for f in range(F):
                    nc.gpsimd.indirect_dma_start(
                        emb[s][:, f, :], None, table_rows,
                        bass.IndirectOffsetOnAxis(ap=idx_stage[:, s, f:f + 1], axis=0)).then_inc(gathered[s], 16)

            gather_tile(0, 0, True)
            gather_tile(0, 1, True)
            with pool.Fori(1, TILES // 2) as j:
                gather_tile(j, 0, False)
                gather_tile(j, 1, False)

        @block.tensor
        def _(pe):
            pe.wait_ge(ident_ready, 1)
            pe.wait_ge(inner_split, 1)
            for h in range(OH):
                last = nc.tensor.transpose(turned[0][0:K, h * P:(h + 1) * P],
                                           inner_parts[:, h, :, :].rearrange("p c f -> p (c f)"), ident[:, :])
            last.then_inc(inner_turned, 1)
            pe.wait_ge(small_loaded, 16 * 5)
            for h in range(OH):
                last = nc.tensor.matmul(bias_ps, w1_sb[:, h, :], lin_b_sb[:, h:h + 1],
                                        start=(h == 0), stop=(h == OH - 1))
            last.then_inc(bias_done, 1)
            pe.wait_ge(lin_loaded, 16)

            def fold_products(i):
                pe.wait_ge(linT_ready, i + 1)
                for g in range(2):
                    for h in range(OH):
                        nc_last = nc.tensor.matmul(head[1][0:R, (2 * i + g) * HID:(2 * i + g + 1) * HID],
                                                   linT[:, i % 2, g, h, :], w1_sb[:, h, :],
                                                   start=(h == 0), stop=(h == OH - 1))
                nc_last.then_inc(fold_done, 1)

            for i in range(EG // 2):
                if i >= 2:
                    pe.wait_ge(linT_ready, i - 1)
                for g in range(2):
                    for h in range(OH):
                        c = (g * OH + h) * P
                        last = nc.tensor.transpose(delta[i % 2][:, c:c + R],
                                                   lin_sb[:, 2 * i + g, h::OH], ident[0:R, 0:R])
                last.then_inc(lin_turned, 1)
                if i >= 1:
                    fold_products(i - 1)
            fold_products(EG // 2 - 1)
            pe.wait_ge(fold_ready, 1)
            pe.wait_ge(bias_ready, 1)
            pe.wait_ge(innerT_ready, 1)

            def turn_tile(j, s):
                pe.wait_ge(gathered[s], (j + 1) * GATHER)
                for k in range(GRPS):
                    if k >= 2:
                        pe.wait_ge(low_ready, count(j, s, GRPS, k - 1))
                    for g in range(GRP):
                        last = nc.tensor.transpose(
                            turned[k % 2][0:R, g * P:(g + 1) * P],
                            emb[s][:, :, :].rearrange("p f e -> p (f e)")[:, k * GRP + g::EG], ident[:, :])
                    last.then_inc(tile_turned, 1)

            def delta_step(j, s, step):
                chunk, e0 = step // CH_STEPS, step % CH_STEPS * STEP_E
                m, h = chunk // OH, chunk % OH
                if step % (OH * CH_STEPS) == 0:
                    pe.wait_ge(regrouped[s][m], (j + 1) * REGROUP)
                if step >= 2:
                    pe.wait_ge(squared, count(j, s, STEPS, step - 1))
                for i in range(2):
                    e = m * E // 2 + e0 + i * GRP
                    last = nc.tensor.matmul(delta[step % 2][:, i * BANK:(i + 1) * BANK], innerT[:, h, :],
                                            emb_parts[s][:, e:e + GRP, :].rearrange("k e b -> k (e b)"),
                                            start=True, stop=True)
                last.then_inc(delta_done, 1)

            def linear_part(s, g):
                for part, (w, x) in enumerate(((fold_lo, emb_lo), (fold_lo, emb_hi), (fold_hi, emb_lo),
                                               (fold_hi, emb_hi))):
                    last = nc.tensor.matmul(pre_h[s], w[:, g, :], x[s][:, g, :],
                                            start=(g == 0 and part == 0), stop=False)
                return last

            def finish_lp(j, s):
                pe.wait_ge(lp_ready, count(j, s, OH, OH))
                for h in range(OH):
                    last = nc.tensor.matmul(pre_h[s], w1_sb[:, OH + h, :], lp[:, s, h, :],
                                            start=False, stop=(h == OH - 1))
                last.then_inc(pre_h_done, 1)

            def finish_y(j, s):
                pe.wait_ge(hid_ready, count(j, s, 1, 1))
                nc.tensor.matmul(y_ps[s], hid[:, s, :], w2_sb[:, :], start=True, stop=True).then_inc(y_done, 1)

            def tile(j, s, before):
                turn_tile(j, s)
                for step in range(STEPS):
                    delta_step(j, s, step)
                    last = linear_part(s, step)
                    if step == STEPS - 1:
                        last.then_inc(linear_done, 1)
                    if before is not None and step == 4:
                        finish_lp(*before)
                    if before is not None and step == 8:
                        finish_y(*before)

            tile(0, 0, None)
            tile(0, 1, (0, 0))
            with pe.Fori(1, TILES // 2) as j:
                tile(j, 0, (j - 1, 1))
                tile(j, 1, (j, 0))
            finish_lp(TILES // 2 - 1, 1)
            finish_y(TILES // 2 - 1, 1)

        @block.scalar
        def _(act):
            act.wait_ge(inner_turned, 1)
            nc.scalar.copy(innerT[:, :, :].rearrange("k h o -> k (h o)"),
                           turned[0][0:K, 0:OH * P]).then_inc(innerT_ready, 1)
            for i in range(EG // 2):
                act.wait_ge(lin_turned, i + 1)
                if i >= 2:
                    act.wait_ge(fold_done, i - 1)
                nc.scalar.copy(linT[:, i % 2, :, :, :].rearrange("p g h c -> p (g h) c"),
                               delta[i % 2][:, 0:2 * OH * P].rearrange("p (n c) -> p n c", c=P)[:, :, 0:R]).then_inc(linT_ready, 1)

            def keep_turned(j, s, k):
                act.wait_ge(tile_turned, count(j, s, GRPS, k + 1))
                nc.scalar.copy(emb_hi[s][:, k * GRP:(k + 1) * GRP, :].rearrange("r g b -> r (g b)"),
                               turned[k % 2][0:R, :]).then_inc(high_ready, 1)

            def square_step(j, s, step, first_tile):
                chunk = step // CH_STEPS
                act.wait_ge(delta_done, count(j, s, STEPS, step + 1))
                if not first_tile and step % CH_STEPS == 0:
                    act.wait_ge(chunk_summed, count(j, s, CHUNKS, chunk + 1 - CHUNKS))
                c = step % CH_STEPS * STEP_COLS
                nc.scalar.activation(squares[:, chunk, c:c + STEP_COLS], delta[step % 2][:, :],
                                     ACT.Square).then_inc(squared, 1)

            def root(j, s, h):
                act.wait_ge(half_summed, count(j, s, OH, h + 1))
                nc.scalar.activation(lp[:, s, h, :], sq_sum[:, h, :], ACT.Sqrt).then_inc(lp_ready, 1)

            def tile(j, s, before, first_use):
                if not first_use:
                    act.wait_ge(linear_done, count(j, s, 1, -1))
                for k in range(GRPS):
                    keep_turned(j, s, k)
                if before is not None:
                    root(*before, OH - 1)
                for step in range(STEPS):
                    square_step(j, s, step, before is None)
                    if step == STEPS - 2:
                        if not first_use:
                            act.wait_ge(pre_h_done, count(j, s, 1, -1))
                        root(j, s, 0)

            tile(0, 0, None, True)
            tile(0, 1, (0, 0), True)
            with act.Fori(1, TILES // 2) as j:
                tile(j, 0, (j - 1, 1), False)
                tile(j, 1, (j, 0), False)
            root(TILES // 2 - 1, 1, OH - 1)
            act.wait_ge(y_kept, TILES)
            nc.scalar.activation(y_sig[:, :], y_all[:, :], ACT.Sigmoid).then_inc(sig_ready, 1)

        @block.vector
        def _(dve):
            dve.wait_ge(idx_loaded, 16)
            nc.vector.tensor_scalar(idx_lim[:, :], idx_raw[:, :], -V, V - 1, ALU.max, ALU.min).then_inc(idx_limited, 1)
            dve.wait_ge(idx_limited, 1)
            nc.vector.tensor_scalar(idx_neg[:, :], idx_lim[:, :], 0, V, ALU.is_lt, ALU.mult).then_inc(idx_based, 1)
            dve.wait_ge(idx_based, 1)
            nc.vector.tensor_tensor(idx_lim[:, :], idx_lim[:, :], idx_neg[:, :], ALU.add).then_inc(idx_based, 1)
            dve.wait_ge(idx_based, 2)
            dve.wait_ge(feat_ready, 1)
            nc.vector.tensor_tensor(idx_row[:, :, :].rearrange("p t f -> p (t f)"), idx_lim[:, :],
                                    feat_row[:, :], ALU.add).then_inc(rows_ready, 1)
            dve.wait_ge(rows_ready, 1)
            for s in range(2):
                nc.vector.tensor_copy(idx_stage[:, s, :], idx_row[:, s, :]).then_inc(staged, 1)
            nc.vector.memset(hid[HID:HID + 1, :, :], 1.0).then_inc(ones_ready, 1)
            dve.wait_ge(inner_loaded, 16)
            for part in range(2):
                last = nc.vector.tensor_copy(inner_parts[:, :, part, :].bitcast(fp32r), inner_sb[:, :, :])
            last.then_inc(inner_high, 1)
            dve.wait_ge(inner_high, 1)
            for part in range(2, PARTS):
                last = nc.vector.tensor_tensor(inner_parts[:, :, part, :], inner_sb[:, :, :], inner_parts[:, :, 0, :],
                                               ALU.subtract)
            last.then_inc(inner_split, 1)
            dve.wait_ge(bias_done, 1)
            nc.vector.tensor_tensor(hid_bias[:, :], bias_ps, b1_sb[:, :], ALU.add).then_inc(bias_ready, 1)
            dve.wait_ge(fold_done, EG // 2)
            nc.vector.tensor_copy(fold_hi[:, :, :].rearrange("r g n -> r (g n)"),
                                  head[1][0:R, 0:EG * HID]).then_inc(fold_high, 1)
            dve.wait_ge(fold_high, 1)
            nc.vector.tensor_tensor(fold_lo[:, :, :].rearrange("r g n -> r (g n)"), head[1][0:R, 0:EG * HID],
                                    fold_hi[:, :, :].bitcast(fp32).rearrange("r g n -> r (g n)"),
                                    ALU.subtract).then_inc(fold_ready, 1)
            dve.wait_ge(bias_ready, 1)

            def sum_chunk(j, s, chunk, first_tile):
                dve.wait_ge(squared, count(j, s, STEPS, CH_STEPS * (chunk + 1)))
                nc.vector.tensor_reduce(part_sum[:, chunk, :], squares[:, chunk, :].rearrange("p (e b) -> p b e", b=P),
                                        AX_X, ALU.add).then_inc(chunk_summed, 1)
                if chunk >= OH:
                    h = chunk - OH
                    dve.wait_ge(chunk_summed, count(j, s, CHUNKS, chunk + 1))
                    if not first_tile:
                        dve.wait_ge(lp_ready, count(j, s, OH, h + 1 - OH))
                    nc.vector.tensor_tensor(sq_sum[:, h, :], part_sum[:, h, :], part_sum[:, chunk, :],
                                            ALU.add).then_inc(half_summed, 1)

            def relu(j, s):
                dve.wait_ge(pre_h_done, count(j, s, 1, 1))
                nc.vector.tensor_scalar(hid[0:HID, s, :], pre_h[s], hid_bias[:, :], 0.0,
                                        ALU.add, ALU.max).then_inc(hid_ready, 1)

            def keep_y(j, s):
                dve.wait_ge(y_done, count(j, s, 1, 1))
                nc.vector.tensor_copy(y_all[:, bass.ds(count(j, s, 1, 0), 1)], y_ps[s]).then_inc(y_kept, 1)

            def split_turned(j, s, k):
                dve.wait_ge(high_ready, count(j, s, GRPS, k + 1))
                cols = slice(k * GRP, (k + 1) * GRP)
                nc.vector.tensor_tensor(emb_lo[s][:, cols, :].rearrange("r g b -> r (g b)"), turned[k % 2][0:R, :],
                                        emb_hi[s][:, cols, :].bitcast(fp32).rearrange("r g b -> r (g b)"),
                                        ALU.subtract).then_inc(low_ready, 1)

            def tile(j, s, before, stage_next):
                for k in range(GRPS):
                    split_turned(j, s, k)
                if stage_next:
                    dve.wait_ge(gathered[s], (j + 1) * GATHER)
                    nc.vector.tensor_copy(idx_stage[:, s, :],
                                          idx_row[:, bass.ds(count(j, s, 1, 2), 1), :].rearrange("p t f -> p (t f)")
                                          ).then_inc(staged, 1)
                for chunk in range(CHUNKS):
                    sum_chunk(j, s, chunk, before is None)
                    if chunk == 1 and before is not None:
                        relu(*before)
                    if chunk == 2 and before is not None:
                        keep_y(*before)

            tile(0, 0, None, True)
            tile(0, 1, (0, 0), True)
            with dve.Fori(1, TILES // 2 - 1) as j:
                tile(j, 0, (j - 1, 1), True)
                tile(j, 1, (j, 0), True)
            last_pair = TILES // 2 - 1
            tile(last_pair, 0, (last_pair - 1, 1), False)
            tile(last_pair, 1, (last_pair, 0), False)
            relu(last_pair, 1)
            keep_y(last_pair, 1)


_INS = ['r_inputs', 'L0_rec_tables', 'L0_rec_lin_w', 'L0_rec_lin_b', 'L0_rec_inner_w',
        'L0_rec_w1', 'L0_rec_b1', 'L0_rec_w2', 'L0_rec_b2']
_OUTS = [((2048, 1), 'float32')]


def kernel(**inputs):
    import numpy as _np
    import concourse.bacc as _bacc
    from concourse import mybir as _mybir
    from concourse.bass_utils import run_bass_kernel_spmd as _run

    nc = _bacc.Bacc("TRN2", target_bir_lowering=False, num_devices=1)
    arrays, args = {}, []
    for name in _INS:
        a = _np.ascontiguousarray(inputs[name])
        arrays[f"in_{name}_dram"] = a
        args.append(nc.dram_tensor(f"in_{name}_dram", a.shape, _mybir.dt.from_np(a.dtype), kind="ExternalInput").ap())
    for i, (shape, dtype) in enumerate(_OUTS):
        dt = _mybir.dt.from_np(_np.dtype(dtype))
        args.append(nc.dram_tensor(f"out_{i}_dram", shape, dt, kind="ExternalOutput").ap())
    product_network_kernel(nc, *args)
    r = _run(nc, [arrays], core_ids=[0])
    return r.results[0]["out_0_dram"]
```

```python
import concourse.bass as bass
from concourse import mybir
from collections import namedtuple
from contextlib import ExitStack

Plan = namedtuple("Plan", "turn low root lp relu y keep_y")


def product_network_kernel(
    nc: bass.Bass,
    r_inputs: bass.AP,
    tables: bass.AP,
    lin_w: bass.AP,
    lin_b: bass.AP,
    inner_w: bass.AP,
    w1: bass.AP,
    b1: bass.AP,
    w2: bass.AP,
    b2: bass.AP,
    out: bass.AP,
):
    fp32 = mybir.dt.float32
    fp32r = mybir.dt.float32r
    i32 = mybir.dt.int32
    u32 = mybir.dt.uint32
    ALU = mybir.AluOpType
    ACT = mybir.ActivationFunctionType
    AX_X = mybir.AxisListType.X

    B, F = r_inputs.shape
    _, V, E = tables.shape
    O = inner_w.shape[0]
    HID = w1.shape[1]
    P = 128
    TILES = B // P
    Q = 4
    EG = E // Q
    R = F * Q
    PARTS = 4
    K = PARTS * F
    OH = O // P
    BANK = 512
    GRP = BANK // P
    GRPS = EG // GRP
    STEP_COLS = 2 * BANK
    STEP_E = 2 * GRP
    RUN = E // 2 // STEP_E
    STEPS = 2 * OH * RUN
    SUM_STEPS = 2
    SUMS = STEPS // SUM_STEPS
    PARTIAL = SUMS // OH
    LAST = TILES // 2 - 1
    GATHER = 16 * F
    REGROUP = 16 * PARTS

    USUAL = Plan(turn=8, low=4, root=6, lp=10, relu=5, y=13, keep_y=7)
    BUT_LAST = Plan(turn=11, low=4, root=6, lp=10, relu=5, y=13, keep_y=7)
    FINAL = Plan(turn=None, low=None, root=6, lp=8, relu=5, y=14, keep_y=7)

    table_rows = tables.rearrange("f v e -> (f v) e")
    idx_dram = r_inputs.rearrange("(p t) f -> p (t f)", p=P)
    out_dram = out.rearrange("(p t) o -> p (t o)", p=P)
    lin_dram = lin_w.rearrange("(r g) o -> r g o", g=EG)

    ctx = ExitStack()
    with ctx:
        def sb(name, shape, dt=fp32):
            return ctx.enter_context(nc.sbuf_tensor(name, shape, dt))

        def sem(name):
            return ctx.enter_context(nc.semaphore(name))

        idx_raw = sb("idx_raw", [P, TILES * F], i32)
        idx_lim = sb("idx_lim", [P, TILES * F])
        idx_neg = sb("idx_neg", [P, TILES * F])
        idx_pos = sb("idx_pos", [P, TILES * F])
        idx_row = sb("idx_row", [P, TILES, F], u32)
        feat_row = sb("feat_row", [P, TILES * F], i32)
        idx_stage = sb("idx_stage", [P, 2, F], u32)
        emb = [sb(f"emb{s}", [P, F, E]) for s in range(2)]
        emb_hi = [sb(f"emb_hi{s}", [R, EG, P], fp32r) for s in range(2)]
        emb_lo = [sb(f"emb_lo{s}", [R, EG, P], fp32r) for s in range(2)]
        emb_parts = [sb(f"emb_parts{s}", [K, E, P], fp32r) for s in range(2)]
        squares = sb("squares", [P, STEPS, STEP_COLS])
        part_sum = sb("part_sum", [P, OH, PARTIAL, P])
        sq_sum = sb("sq_sum", [P, OH, P])
        lp = sb("lp", [P, 2, OH, P])
        hid = sb("hid", [HID + 1, 2, P])
        y_all = sb("y_all", [P, TILES - 1])
        y_sig = sb("y_sig", [P, TILES])
        ident = sb("ident", [P, P])
        inner_sb = sb("inner_sb", [P, OH, F])
        inner_parts = sb("inner_parts", [P, OH, PARTS, F])
        innerT = sb("innerT", [K, OH, P], fp32r)
        lin_sb = squares[0:R, 0:EG * O // STEP_COLS, :].rearrange("r s (g o) -> r (s g) o", o=O)
        linT = sb("linT", [P, 2, 2, OH, R])
        fold_hi = sb("fold_hi", [R, EG, HID], fp32r)
        fold_lo = sb("fold_lo", [R, EG, HID], fp32r)
        w1_sb = sb("w1_sb", [P, 2 * OH, HID])
        lin_b_sb = sb("lin_b_sb", [P, OH])
        b1_sb = sb("b1_sb", [HID, 1])
        hid_bias = sb("hid_bias", [HID, 1])
        w2_sb = sb("w2_sb", [HID + 1, 1])

        delta = [ctx.enter_context(nc.psum_tensor(f"delta{i}", [P, STEP_COLS], fp32)) for i in range(2)]
        turned = [ctx.enter_context(nc.psum_tensor(f"turned{i}", [P, BANK], fp32)) for i in range(2)]
        head = [ctx.enter_context(nc.psum_tensor(f"head{i}", [P, BANK], fp32)) for i in range(2)]
        pre_h = [head[s][0:HID, 0:P] for s in range(2)]
        y_ps = [head[s][:, P:P + 1] for s in range(2)]
        bias_ps = head[0][0:HID, 0:1]

        idx_loaded = [sem(f"idx_loaded{i}") for i in range(2)]
        inner_loaded = sem("inner_loaded")
        lin_loaded = sem("lin_loaded")
        small_loaded = sem("small_loaded")
        feat_ready = sem("feat_ready")
        ident_ready = sem("ident_ready")
        ident_zero = sem("ident_zero")
        idx_limited = sem("idx_limited")
        idx_based = sem("idx_based")
        idx_positive = sem("idx_positive")
        rows_ready = sem("rows_ready")
        inner_high = sem("inner_high")
        inner_split = sem("inner_split")
        inner_turned = sem("inner_turned")
        innerT_ready = sem("innerT_ready")
        lin_turned = sem("lin_turned")
        linT_ready = sem("linT_ready")
        fold_done = sem("fold_done")
        fold_high = sem("fold_high")
        fold_ready = sem("fold_ready")
        bias_done = sem("bias_done")
        bias_ready = sem("bias_ready")
        ones_ready = sem("ones_ready")
        staged = sem("staged")
        gather_begun = sem("gather_begun")
        gathered = [sem(f"gathered{s}") for s in range(2)]
        tile_turned = sem("tile_turned")
        high_ready = sem("high_ready")
        low_ready = sem("low_ready")
        regrouped = [[sem(f"regrouped{s}_{q}") for q in range(Q)] for s in range(2)]
        regrouped_pool = [sem(f"regrouped_pool_{q}") for q in range(Q)]
        delta_done = sem("delta_done")
        squared = sem("squared")
        part_summed = sem("part_summed")
        folded = sem("folded")
        pool_summed = sem("pool_summed")
        half_summed = sem("half_summed")
        lp_ready = sem("lp_ready")
        linear_done = sem("linear_done")
        pre_h_done = sem("pre_h_done")
        hid_ready = sem("hid_ready")
        y_done = sem("y_done")
        y_kept = sem("y_kept")
        sig_ready = sem("sig_ready")
        out_stored = sem("out_stored")

        def count(j, s, each, more):
            return j * (2 * each) + (s * each + more)

        def regroup(eng, s, q, part):
            src = (emb_hi, emb_lo)[part % 2][s]
            return eng.dma_start(emb_parts[s][part * F:(part + 1) * F, q * EG:(q + 1) * EG, :].bitcast(fp32),
                                 src[q::Q, :, :].bitcast(fp32))

        SP_PARTS = ((0, 1, 2), (0, 1), (0, 1, 2), (0, 1))
        POOL_PARTS = ((3,), (2, 3), (3,), (2, 3))

        POOL_SUMS = {(LAST, 0): (4,), (LAST, 1): (1, 5)}

        def place(n):
            run = n * SUM_STEPS // RUN
            return run % OH, run // OH * (PARTIAL // 2) + n % (PARTIAL // 2)

        block = ctx.enter_context(nc.Block())

        @block.sync
        def _(sp):
            sp.dma_start(idx_raw[:, 0:2 * F], idx_dram[:, 0:2 * F]).then_inc(idx_loaded[0], 16)
            sp.dma_start(idx_raw[:, 2 * F:], idx_dram[:, 2 * F:]).then_inc(idx_loaded[1], 16)
            sp.dma_start(inner_sb[:, :, :], inner_w.rearrange("(p h) f -> p h f", h=OH)).then_inc(inner_loaded, 16)
            sp.dma_start(w1_sb[:, :, :].rearrange("p (c h) n -> p c h n", h=OH),
                         w1.rearrange("(c p h) n -> p c h n", p=P, h=OH)).then_inc(small_loaded, 16)
            sp.dma_start(lin_b_sb[:, :], lin_b.rearrange("(p h) -> p h", h=OH)).then_inc(small_loaded, 16)
            sp.dma_start(b1_sb[:, :], b1.rearrange("(p o) -> p o", o=1)).then_inc(small_loaded, 16)
            sp.dma_start(w2_sb[0:HID, :], w2).then_inc(small_loaded, 16)
            sp.dma_start(w2_sb[HID:HID + 1, :], b2.rearrange("(p o) -> p o", o=1)).then_inc(small_loaded, 16)
            sp.dma_start(lin_sb[:, :, :], lin_dram).then_inc(lin_loaded, 16)

            def regroup_tile(j, s, first_use, parts=(range(PARTS),) * Q, early=()):
                if early:
                    sp.wait_ge(high_ready, count(j, s, GRPS, GRPS))
                    sp.wait_ge(delta_done, count(j, s, STEPS, -STEPS))
                    for part in early:
                        regroup(sp, s, 0, part).then_inc(regrouped[s][0], 16)
                sp.wait_ge(low_ready, count(j, s, GRPS, GRPS))
                if not first_use and not early:
                    sp.wait_ge(delta_done, count(j, s, STEPS, -STEPS))
                for q in range(Q):
                    for part in parts[q]:
                        if q > 0 or part not in early:
                            regroup(sp, s, q, part).then_inc(regrouped[s][q], 16)

            regroup_tile(0, 0, True)
            regroup_tile(0, 1, True)
            with sp.Fori(1, LAST) as j:
                regroup_tile(j, 0, False)
                regroup_tile(j, 1, False)
            regroup_tile(LAST, 0, False)
            regroup_tile(LAST, 1, False, SP_PARTS, early=(0, 2))
            sp.wait_ge(sig_ready, 2)
            sp.dma_start(out_dram, y_sig[:, :]).then_inc(out_stored, 16)
            sp.wait_ge(out_stored, 16)

        @block.gpsimd
        def _(pool):
            nc.gpsimd.iota(feat_row[:, :].rearrange("p (t f) -> p t f", f=F), [[0, TILES], [V, F]],
                           base=0, channel_multiplier=0).then_inc(feat_ready, 1)
            nc.gpsimd.memset(ident[:, :], 0.0).then_inc(ident_zero, 1)
            pool.wait_ge(ident_zero, 1)
            nc.gpsimd.affine_select(out=ident[:, :], in_=ident[:, :], compare_op=ALU.not_equal, fill=1.0,
                                    base=0, pattern=[[-1, P]], channel_multiplier=1).then_inc(ident_ready, 1)

            def gather_tile(j, s, first_use):
                pool.wait_ge(staged, count(j, s, 1, 1))
                if not first_use:
                    pool.wait_ge(tile_turned, count(j, s, GRPS, -GRPS))
                pool.sem_inc(gather_begun, 1)
                for f in range(F):
                    nc.gpsimd.indirect_dma_start(
                        emb[s][:, f, :], None, table_rows,
                        bass.IndirectOffsetOnAxis(ap=idx_stage[:, s, f:f + 1], axis=0)).then_inc(gathered[s], 16)

            gather_tile(0, 0, True)
            gather_tile(0, 1, True)
            with pool.Fori(1, TILES // 2) as j:
                gather_tile(j, 0, False)
                gather_tile(j, 1, False)

            folds = [0]

            def sum_squares(j, s, n):
                h, k = place(n)
                pool.wait_ge(squared, count(j, s, STEPS, SUM_STEPS * (n + 1)))
                sq = squares[:, n * SUM_STEPS:(n + 1) * SUM_STEPS, :].rearrange("p s c -> p (s c)")
                cols = SUM_STEPS * STEP_COLS // 2
                while cols > P:
                    nc.gpsimd.tensor_tensor(sq[:, 0:cols], sq[:, 0:cols], sq[:, cols:2 * cols],
                                            ALU.add).then_inc(folded, 1)
                    folds[0] += 1
                    pool.wait_ge(folded, folds[0])
                    cols //= 2
                nc.gpsimd.tensor_tensor(part_sum[:, h, k, :], sq[:, 0:P], sq[:, P:2 * P],
                                        ALU.add).then_inc(pool_summed, 1)

            pool.wait_ge(half_summed, LAST * 2 * OH)
            for n in POOL_SUMS[LAST, 0]:
                sum_squares(LAST, 0, n)
            pool.wait_ge(low_ready, TILES * GRPS)
            for q in range(Q):
                for part in POOL_PARTS[q]:
                    regroup(nc.gpsimd, 1, q, part).then_inc(regrouped_pool[q], 16)
            pool.wait_ge(half_summed, (LAST * 2 + 1) * OH)
            for n in POOL_SUMS[LAST, 1]:
                sum_squares(LAST, 1, n)

        @block.tensor
        def _(pe):
            pe.wait_ge(ident_ready, 1)
            pe.wait_ge(inner_split, 1)
            for h in range(OH):
                last = nc.tensor.transpose(turned[0][0:K, h * P:(h + 1) * P],
                                           inner_parts[:, h, :, :].rearrange("p c f -> p (c f)"), ident[:, :])
            last.then_inc(inner_turned, 1)
            pe.wait_ge(small_loaded, 16 * 5)
            for h in range(OH):
                last = nc.tensor.matmul(bias_ps, w1_sb[:, h, :], lin_b_sb[:, h:h + 1],
                                        start=(h == 0), stop=(h == OH - 1))
            last.then_inc(bias_done, 1)
            pe.wait_ge(lin_loaded, 16)

            def fold_products(i):
                pe.wait_ge(linT_ready, i + 1)
                for g in range(2):
                    for h in range(OH):
                        nc_last = nc.tensor.matmul(head[1][0:R, (2 * i + g) * HID:(2 * i + g + 1) * HID],
                                                   linT[:, i % 2, g, h, :], w1_sb[:, h, :],
                                                   start=(h == 0), stop=(h == OH - 1))
                nc_last.then_inc(fold_done, 1)

            for i in range(EG // 2):
                if i >= 2:
                    pe.wait_ge(linT_ready, i - 1)
                for g in range(2):
                    for h in range(OH):
                        c = (g * OH + h) * P
                        last = nc.tensor.transpose(delta[i % 2][:, c:c + R],
                                                   lin_sb[:, 2 * i + g, h::OH], ident[0:R, 0:R])
                last.then_inc(lin_turned, 1)
                if i >= 1:
                    fold_products(i - 1)
            fold_products(EG // 2 - 1)
            pe.wait_ge(fold_ready, 1)
            pe.wait_ge(bias_ready, 1)
            pe.wait_ge(innerT_ready, 1)

            def turn_tile(j, s):
                pe.wait_ge(gathered[s], (j + 1) * GATHER)
                for k in range(GRPS):
                    if k >= 2:
                        pe.wait_ge(low_ready, count(j, s, GRPS, k - 1))
                    for g in range(GRP):
                        last = nc.tensor.transpose(
                            turned[k % 2][0:R, g * P:(g + 1) * P],
                            emb[s][:, :, :].rearrange("p f e -> p (f e)")[:, k * GRP + g::EG], ident[:, :])
                    last.then_inc(tile_turned, 1)

            def delta_step(j, s, step, first_tile, last_tile):
                run, e0 = step // RUN, step % RUN * STEP_E
                m, h = run // OH, run % OH
                q, first_e = divmod(m * E // 2 + e0, EG)
                if h == 0 and first_e == 0:
                    if last_tile:
                        pe.wait_ge(regrouped_pool[q], 16 * len(POOL_PARTS[q]))
                        pe.wait_ge(regrouped[s][q], j * REGROUP + 16 * len(SP_PARTS[q]))
                    else:
                        pe.wait_ge(regrouped[s][q], (j + 1) * REGROUP)
                if step >= 2 or not first_tile:
                    pe.wait_ge(squared, count(j, s, STEPS, step - 1))
                for i in range(2):
                    e = m * E // 2 + e0 + i * GRP
                    last = nc.tensor.matmul(delta[step % 2][:, i * BANK:(i + 1) * BANK], innerT[:, h, :],
                                            emb_parts[s][:, e:e + GRP, :].rearrange("k e b -> k (e b)"),
                                            start=True, stop=True)
                last.then_inc(delta_done, 1)

            def linear_part(s, g):
                for part, (w, x) in enumerate(((fold_lo, emb_lo), (fold_lo, emb_hi), (fold_hi, emb_lo),
                                               (fold_hi, emb_hi))):
                    last = nc.tensor.matmul(pre_h[s], w[:, g, :], x[s][:, g, :],
                                            start=(g == 0 and part == 0), stop=False)
                return last

            def finish_lp(j, s):
                pe.wait_ge(lp_ready, count(j, s, 1, 1))
                for h in range(OH):
                    last = nc.tensor.matmul(pre_h[s], w1_sb[:, OH + h, :], lp[:, s, h, :],
                                            start=False, stop=(h == OH - 1))
                last.then_inc(pre_h_done, 1)

            def finish_y(j, s):
                pe.wait_ge(hid_ready, count(j, s, 1, 1))
                nc.tensor.matmul(y_ps[s], hid[:, s, :], w2_sb[:, :], start=True, stop=True).then_inc(y_done, 1)

            def tile(j, s, before, after, plan=USUAL, first_use=False):
                for step in range(STEPS):
                    if before is not None and step == plan.lp:
                        finish_lp(*before)
                    if before is not None and step == plan.y:
                        finish_y(*before)
                    if after is not None and step == plan.turn:
                        turn_tile(*after)
                    delta_step(j, s, step, before is None, after is None)
                    if step == 0 and not first_use:
                        pe.wait_ge(y_kept, count(j, s, 1, -1))
                    last = linear_part(s, step)
                last.then_inc(linear_done, 1)

            turn_tile(0, 0)
            tile(0, 0, None, (0, 1), first_use=True)
            tile(0, 1, (0, 0), (1, 0), first_use=True)
            with pe.Fori(1, LAST) as j:
                tile(j, 0, (j - 1, 1), (j, 1))
                tile(j, 1, (j, 0), (j + 1, 0))
            tile(LAST, 0, (LAST - 1, 1), (LAST, 1), BUT_LAST)
            tile(LAST, 1, (LAST, 0), None, FINAL)
            finish_lp(LAST, 1)
            finish_y(LAST, 1)

        @block.scalar
        def _(act):
            act.wait_ge(inner_turned, 1)
            nc.scalar.copy(innerT[:, :, :].rearrange("k h o -> k (h o)"),
                           turned[0][0:K, 0:OH * P]).then_inc(innerT_ready, 1)
            for i in range(EG // 2):
                act.wait_ge(lin_turned, i + 1)
                if i >= 2:
                    act.wait_ge(fold_done, i - 1)
                nc.scalar.copy(linT[:, i % 2, :, :, :].rearrange("p g h c -> p (g h) c"),
                               delta[i % 2][:, 0:2 * OH * P].rearrange("p (n c) -> p n c", c=P)[:, :, 0:R]).then_inc(linT_ready, 1)

            def keep_turned(j, s, first_use):
                if not first_use:
                    act.wait_ge(linear_done, count(j, s, 1, -1))
                for k in range(GRPS):
                    act.wait_ge(tile_turned, count(j, s, GRPS, k + 1))
                    nc.scalar.copy(emb_hi[s][:, k * GRP:(k + 1) * GRP, :].rearrange("r g b -> r (g b)"),
                                   turned[k % 2][0:R, :]).then_inc(high_ready, 1)

            def square_step(j, s, step, first_tile, pools_before):
                act.wait_ge(delta_done, count(j, s, STEPS, step + 1))
                n = step // SUM_STEPS
                if not first_tile and step % SUM_STEPS == 0:
                    if n in pools_before:
                        act.wait_ge(pool_summed, pools_before.index(n) + 1)
                    else:
                        own = n + 1 - SUMS - sum(m < n for m in pools_before)
                        act.wait_ge(part_summed, count(j, s, SUMS, own))
                nc.scalar.activation(squares[:, step, :], delta[step % 2][:, :], ACT.Square).then_inc(squared, 1)

            def root(j, s, first_use):
                act.wait_ge(half_summed, count(j, s, OH, OH))
                if not first_use:
                    act.wait_ge(pre_h_done, count(j, s, 1, -1))
                nc.scalar.activation(lp[:, s, :, :].rearrange("p h b -> p (h b)"),
                                     sq_sum[:, :, :].rearrange("p h b -> p (h b)"), ACT.Sqrt).then_inc(lp_ready, 1)

            def tile(j, s, before, after, plan=USUAL, pools_before=()):
                for step in range(STEPS):
                    if before is not None and step == plan.root:
                        root(*before)
                    if after is not None and step == plan.turn:
                        keep_turned(*after)
                    square_step(j, s, step, before is None, pools_before)

            keep_turned(0, 0, True)
            tile(0, 0, None, (0, 1, True))
            tile(0, 1, (0, 0, True), (1, 0, False))
            tile(1, 0, (0, 1, True), (1, 1, False))
            tile(1, 1, (1, 0, False), (2, 0, False))
            with act.Fori(2, LAST) as j:
                tile(j, 0, (j - 1, 1, False), (j, 1, False))
                tile(j, 1, (j, 0, False), (j + 1, 0, False))
            tile(LAST, 0, (LAST - 1, 1, False), (LAST, 1, False), BUT_LAST)
            tile(LAST, 1, (LAST, 0, False), None, FINAL, pools_before=POOL_SUMS[LAST, 0])
            root(LAST, 1, False)
            act.wait_ge(y_kept, TILES - 1)
            nc.scalar.activation(y_sig[:, 0:TILES - 1], y_all[:, :], ACT.Sigmoid).then_inc(sig_ready, 1)
            act.wait_ge(y_done, TILES)
            nc.scalar.activation(y_sig[:, TILES - 1:TILES], y_ps[1], ACT.Sigmoid).then_inc(sig_ready, 1)

        @block.vector
        def _(dve):
            for i, (cols, rows, done) in enumerate((
                    (slice(0, 2 * F), idx_stage[:, :, :].rearrange("p t f -> p (t f)"), staged),
                    (slice(2 * F, TILES * F), idx_row[:, 2:, :].rearrange("p t f -> p (t f)"), rows_ready))):
                dve.wait_ge(idx_loaded[i], 16)
                nc.vector.tensor_scalar(idx_lim[:, cols], idx_raw[:, cols], -V, V - 1,
                                        ALU.max, ALU.min).then_inc(idx_limited, 1)
                dve.wait_ge(idx_limited, i + 1)
                nc.vector.tensor_scalar(idx_neg[:, cols], idx_lim[:, cols], 0, V,
                                        ALU.is_lt, ALU.mult).then_inc(idx_based, 1)
                dve.wait_ge(idx_based, i + 1)
                nc.vector.tensor_tensor(idx_pos[:, cols], idx_lim[:, cols], idx_neg[:, cols],
                                        ALU.add).then_inc(idx_positive, 1)
                dve.wait_ge(idx_positive, i + 1)
                dve.wait_ge(feat_ready, 1)
                nc.vector.tensor_tensor(rows, idx_pos[:, cols], feat_row[:, cols],
                                        ALU.add).then_inc(done, 2 if i == 0 else 1)
            dve.wait_ge(rows_ready, 1)
            nc.vector.memset(hid[HID:HID + 1, :, :], 1.0).then_inc(ones_ready, 1)
            dve.wait_ge(inner_loaded, 16)
            for part in range(2):
                last = nc.vector.tensor_copy(inner_parts[:, :, part, :].bitcast(fp32r), inner_sb[:, :, :])
            last.then_inc(inner_high, 1)
            dve.wait_ge(inner_high, 1)
            for part in range(2, PARTS):
                last = nc.vector.tensor_tensor(inner_parts[:, :, part, :], inner_sb[:, :, :], inner_parts[:, :, 0, :],
                                               ALU.subtract)
            last.then_inc(inner_split, 1)
            dve.wait_ge(bias_done, 1)
            nc.vector.tensor_tensor(hid_bias[:, :], bias_ps, b1_sb[:, :], ALU.add).then_inc(bias_ready, 1)
            dve.wait_ge(fold_done, EG // 2)
            nc.vector.tensor_copy(fold_hi[:, :, :].rearrange("r g n -> r (g n)"),
                                  head[1][0:R, 0:EG * HID]).then_inc(fold_high, 1)
            dve.wait_ge(fold_high, 1)
            nc.vector.tensor_tensor(fold_lo[:, :, :].rearrange("r g n -> r (g n)"), head[1][0:R, 0:EG * HID],
                                    fold_hi[:, :, :].bitcast(fp32).rearrange("r g n -> r (g n)"),
                                    ALU.subtract).then_inc(fold_ready, 1)
            dve.wait_ge(bias_ready, 1)

            own_sums = [(LAST * 2) * SUMS]

            def sum_squares(j, s, n, first_tile, shared, defer):
                h, k = place(n)
                if n == 0 and not first_tile:
                    dve.wait_ge(half_summed, count(j, s, OH, 0))
                if n not in shared:
                    dve.wait_ge(squared, count(j, s, STEPS, SUM_STEPS * (n + 1)))
                    nc.vector.tensor_reduce(part_sum[:, h, k, :],
                                            squares[:, n * SUM_STEPS:(n + 1) * SUM_STEPS, :].rearrange(
                                                "p s (e b) -> p b (s e)", b=P),
                                            AX_X, ALU.add).then_inc(part_summed, 1)
                    if shared:
                        own_sums[0] += 1
                if k == PARTIAL - 1 and not defer:
                    sum_half(j, s, h, n, first_tile, shared)

            def sum_half(j, s, h, n, first_tile, shared):
                if shared:
                    dve.wait_ge(part_summed, own_sums[0])
                    made = sum(len(POOL_SUMS[LAST, i]) for i in range(s))
                    dve.wait_ge(pool_summed, made + sum(place(m)[0] <= h for m in shared))
                else:
                    dve.wait_ge(part_summed, count(j, s, SUMS, n + 1))
                if not first_tile:
                    dve.wait_ge(lp_ready, count(j, s, 1, 0))
                nc.vector.tensor_reduce(sq_sum[:, h, :], part_sum[:, h, :, :].rearrange("p k b -> p b k"),
                                        AX_X, ALU.add).then_inc(half_summed, 1)

            def relu(j, s):
                dve.wait_ge(pre_h_done, count(j, s, 1, 1))
                nc.vector.tensor_scalar(hid[0:HID, s, :], pre_h[s], hid_bias[:, :], 0.0,
                                        ALU.add, ALU.max).then_inc(hid_ready, 1)

            def keep_y(j, s):
                dve.wait_ge(y_done, count(j, s, 1, 1))
                nc.vector.tensor_copy(y_all[:, bass.ds(count(j, s, 1, 0), 1)], y_ps[s]).then_inc(y_kept, 1)

            def split_turned(j, s, stage_next):
                for k in range(GRPS):
                    dve.wait_ge(high_ready, count(j, s, GRPS, k + 1))
                    cols = slice(k * GRP, (k + 1) * GRP)
                    nc.vector.tensor_tensor(emb_lo[s][:, cols, :].rearrange("r g b -> r (g b)"),
                                            turned[k % 2][0:R, :],
                                            emb_hi[s][:, cols, :].bitcast(fp32).rearrange("r g b -> r (g b)"),
                                            ALU.subtract).then_inc(low_ready, 1)
                if stage_next:
                    dve.wait_ge(gathered[s], (j + 1) * GATHER)
                    nc.vector.tensor_copy(idx_stage[:, s, :],
                                          idx_row[:, bass.ds(count(j, s, 1, 2), 1), :].rearrange("p t f -> p (t f)")
                                          ).then_inc(staged, 1)

            def tile(j, s, before, after, plan=USUAL, shared=()):
                for n in range(SUMS):
                    if before is not None and n == plan.relu:
                        relu(*before)
                    if after is not None and n == plan.low:
                        split_turned(*after)
                    if before is not None and n == plan.keep_y:
                        keep_y(*before)
                    sum_squares(j, s, n, before is None, shared, plan.turn is None)
                if plan.turn is None:
                    for h in range(OH):
                        sum_half(j, s, h, SUMS - 1, False, shared)

            split_turned(0, 0, True)
            tile(0, 0, None, (0, 1, True))
            tile(0, 1, (0, 0), (1, 0, True))
            with dve.Fori(1, LAST - 1) as j:
                tile(j, 0, (j - 1, 1), (j, 1, True))
                tile(j, 1, (j, 0), (j + 1, 0, True))
            tile(LAST - 1, 0, (LAST - 2, 1), (LAST - 1, 1, True))
            tile(LAST - 1, 1, (LAST - 1, 0), (LAST, 0, False))
            tile(LAST, 0, (LAST - 1, 1), (LAST, 1, False), BUT_LAST, shared=POOL_SUMS[LAST, 0])
            tile(LAST, 1, (LAST, 0), None, FINAL, shared=POOL_SUMS[LAST, 1])
            relu(LAST, 1)


_INS = ['r_inputs', 'L0_rec_tables', 'L0_rec_lin_w', 'L0_rec_lin_b', 'L0_rec_inner_w',
        'L0_rec_w1', 'L0_rec_b1', 'L0_rec_w2', 'L0_rec_b2']
_OUTS = [((2048, 1), 'float32')]


def kernel(**inputs):
    import numpy as _np
    import concourse.bacc as _bacc
    from concourse import mybir as _mybir
    from concourse.bass_utils import run_bass_kernel_spmd as _run

    nc = _bacc.Bacc("TRN2", target_bir_lowering=False, num_devices=1)
    arrays, args = {}, []
    for name in _INS:
        a = _np.ascontiguousarray(inputs[name])
        arrays[f"in_{name}_dram"] = a
        args.append(nc.dram_tensor(f"in_{name}_dram", a.shape, _mybir.dt.from_np(a.dtype), kind="ExternalInput").ap())
    for i, (shape, dtype) in enumerate(_OUTS):
        dt = _mybir.dt.from_np(_np.dtype(dtype))
        args.append(nc.dram_tensor(f"out_{i}_dram", shape, dt, kind="ExternalOutput").ap())
    product_network_kernel(nc, *args)
    r = _run(nc, [arrays], core_ids=[0])
    return r.results[0]["out_0_dram"]
```
